# Optimizing a Trainium2 kernel written in Bass

```python
import numpy as np
import jax
import jax.numpy as jnp

def _softmax(x, axis=-1):
    return jax.nn.softmax(x, axis=axis)

def _gelu(x):
    return jax.nn.gelu(x, approximate=True)

def _silu(x):
    return jax.nn.silu(x)

def _sigmoid(x):
    return jax.nn.sigmoid(x)

def _layernorm(x, axis=-1, eps=1e-05):
    m = jnp.mean(x, axis=axis, keepdims=True)
    v = jnp.var(x, axis=axis, keepdims=True)
    return (x - m) / jnp.sqrt(v + eps)

def _scatter_add(tgt, idx, src, axis=0):
    return tgt.at[idx].add(src)

def _segment_sum(src, seg, n):
    return jax.ops.segment_sum(src, seg, n)
kernel_name = 'mk_macaron_d2_jaxref_r8_6c8524'

def setup_inputs(seed: int=0):
    np.random.seed(seed)
    _w = jnp.asarray

    def _L0_attn_setup():
        import jax, jax.numpy as jnp
        import numpy as np
        N_HEAD = 32
        ROPE_BASE = 10000.0

        def _rope_cos_sin(T, n_elem, dtype):
            theta = 1.0 / ROPE_BASE ** (jnp.arange(0, n_elem, 2, dtype=dtype) / n_elem)
            seq_idx = jnp.arange(T, dtype=dtype)
            idx_theta = jnp.outer(seq_idx, theta)
            idx_theta2 = jnp.concatenate([idx_theta, idx_theta], axis=-1)
            return (jnp.cos(idx_theta2), jnp.sin(idx_theta2))

        def _apply_rope(x, cos, sin):
            d2 = x.shape[-1] // 2
            rot = jnp.concatenate([-x[..., d2:], x[..., :d2]], axis=-1)
            return x * cos + rot * sin
        key = jax.random.key(seed)
        k1, k2, k3, k4 = jax.random.split(key, 4)
        B, T, C = (1, 256, 512)
        s_in = 1.0 / np.sqrt(C)
        return {'x': jax.random.normal(k1, (B, T, C), jnp.float32), 'w_attn': jax.random.normal(k2, (3 * C, C), jnp.float32) * s_in, 'w_proj': jax.random.normal(k3, (C, C), jnp.float32) * s_in, 'adapter_wte': jax.random.normal(k4, (10, C), jnp.float32), 'gating': jnp.ones((1,), jnp.float32)}
    _L0_attn_in = _L0_attn_setup()

    def _L0_ffn_setup():
        import jax, jax.numpy as jnp
        import numpy as np
        NUM_EXPERTS = 8
        RANK = 32
        ALPHA = 16.0
        TOP_K = 2
        TEMPERATURE = 1.0
        GAMMA = 0.5
        SOFT_TOPK_TEMP = 0.5
        N_GRAM = 2
        EPS = 1e-06
        key = jax.random.key(seed)
        ks = jax.random.split(key, 6)
        d_in, d_out = (512, 512)
        Bsz, T = (4, 256)
        x = jax.random.normal(ks[0], (Bsz, T, d_in), dtype=jnp.float32)
        W = jax.random.normal(ks[1], (d_out, d_in), dtype=jnp.float32) / np.sqrt(d_in)
        b = jax.random.normal(ks[2], (d_out,), dtype=jnp.float32) * 0.01
        A = jax.random.normal(ks[3], (d_in, RANK), dtype=jnp.float32) / np.sqrt(d_in)
        Bmat = jax.random.normal(ks[4], (RANK, d_out), dtype=jnp.float32) * 0.01
        LiMEs = jax.random.normal(ks[5], (NUM_EXPERTS, RANK), dtype=jnp.float32) * 0.1
        return {'x': x, 'W': W, 'b': b, 'A': A, 'Bmat': Bmat, 'LiMEs': LiMEs}
    _L0_ffn_in = _L0_ffn_setup()

    def _L1_attn_setup():
        import jax, jax.numpy as jnp
        import numpy as np
        DIM = 512
        N_HEADS = 32
        N_KV_HEADS = 8
        HEAD_DIM = 128
        B, S = (2, 256)
        key = jax.random.key(seed)
        k1, k2, k3, k4, k5 = jax.random.split(key, 5)
        sc = 0.02
        return {'x': jax.random.normal(k1, (B, S, DIM), dtype=jnp.float32), 'wq': jax.random.normal(k2, (N_HEADS * HEAD_DIM, DIM), dtype=jnp.float32) * sc, 'wk': jax.random.normal(k3, (N_KV_HEADS * HEAD_DIM, DIM), dtype=jnp.float32) * sc, 'wv': jax.random.normal(k4, (N_KV_HEADS * HEAD_DIM, DIM), dtype=jnp.float32) * sc, 'wo': jax.random.normal(k5, (DIM, N_HEADS * HEAD_DIM), dtype=jnp.float32) * sc}
    _L1_attn_in = _L1_attn_setup()

    def _L1_ffn_setup():
        import jax, jax.numpy as jnp
        import numpy as np
        HIDDEN = 512
        MOE_INTER = 128
        SHARED_INTER = 512
        NUM_EXPERTS = 16
        TOP_K = 2

        def _moe_forward(x, gate_w, w_gate_up, w_down, shared_w_gate_up, shared_w_down):
            orig_shape = x.shape
            x2 = x.reshape(-1, orig_shape[-1])
            gu_s = x2 @ shared_w_gate_up.T
            g_s, u_s = jnp.split(gu_s, 2, axis=-1)
            shared_out = jax.nn.silu(g_s) * u_s @ shared_w_down.T
            logits = x2 @ gate_w.T
            probs = jax.nn.softmax(logits, axis=-1)
            topk_vals, topk_idx = jax.lax.top_k(probs, TOP_K)
            topk_vals = topk_vals / jnp.sum(topk_vals, axis=-1, keepdims=True)
            combine = jnp.sum(jax.nn.one_hot(topk_idx, NUM_EXPERTS, dtype=x2.dtype) * topk_vals[..., None], axis=1)
            gu = jnp.einsum('th,eih->eti', x2, w_gate_up)
            g, u = jnp.split(gu, 2, axis=-1)
            act = jax.nn.silu(g) * u
            out_e = jnp.einsum('eti,ehi->eth', act, w_down)
            moe_out = jnp.einsum('eth,te->th', out_e, combine)
            return (moe_out + shared_out).reshape(orig_shape)
        key = jax.random.key(seed)
        ks = jax.random.split(key, 6)
        s = 0.02
        hidden_states = jax.random.normal(ks[0], (2, 256, HIDDEN), dtype=jnp.float32)
        gate_w = jax.random.normal(ks[1], (NUM_EXPERTS, HIDDEN), dtype=jnp.float32) * s
        w_gate_up = jax.random.normal(ks[2], (NUM_EXPERTS, 2 * MOE_INTER, HIDDEN), dtype=jnp.float32) * s
        w_down = jax.random.normal(ks[3], (NUM_EXPERTS, HIDDEN, MOE_INTER), dtype=jnp.float32) * s
        shared_w_gate_up = jax.random.normal(ks[4], (2 * SHARED_INTER, HIDDEN), dtype=jnp.float32) * s
        shared_w_down = jax.random.normal(ks[5], (HIDDEN, SHARED_INTER), dtype=jnp.float32) * s
        return {'hidden_states': hidden_states, 'gate_w': gate_w, 'w_gate_up': w_gate_up, 'w_down': w_down, 'shared_w_gate_up': shared_w_gate_up, 'shared_w_down': shared_w_down}
    _L1_ffn_in = _L1_ffn_setup()
    _d = {'L0_attn_x': _L0_attn_in['x'], 'L0_attn_w_attn': _L0_attn_in['w_attn'], 'L0_attn_w_proj': _L0_attn_in['w_proj'], 'L0_attn_adapter_wte': _L0_attn_in['adapter_wte'], 'L0_attn_gating': _L0_attn_in['gating'], 'L0_ffn_W': _L0_ffn_in['W'], 'L0_ffn_b': _L0_ffn_in['b'], 'L0_ffn_A': _L0_ffn_in['A'], 'L0_ffn_Bmat': _L0_ffn_in['Bmat'], 'L0_ffn_LiMEs': _L0_ffn_in['LiMEs'], 'L1_attn_wq': _L1_attn_in['wq'], 'L1_attn_wk': _L1_attn_in['wk'], 'L1_attn_wv': _L1_attn_in['wv'], 'L1_attn_wo': _L1_attn_in['wo'], 'L1_ffn_gate_w': _L1_ffn_in['gate_w'], 'L1_ffn_w_gate_up': _L1_ffn_in['w_gate_up'], 'L1_ffn_w_down': _L1_ffn_in['w_down'], 'L1_ffn_shared_w_gate_up': _L1_ffn_in['shared_w_gate_up'], 'L1_ffn_shared_w_down': _L1_ffn_in['shared_w_down']}
    _x0 = _d['L0_attn_x']
    _d['L0_attn_x'] = jax.random.normal(jax.random.fold_in(jax.random.key(seed), 1), (2, 512, 512), dtype=_x0.dtype)
    del _x0
    return _d

def reference(L0_attn_x, L0_attn_w_attn, L0_attn_w_proj, L0_attn_adapter_wte, L0_attn_gating, L0_ffn_W, L0_ffn_b, L0_ffn_A, L0_ffn_Bmat, L0_ffn_LiMEs, L1_attn_wq, L1_attn_wk, L1_attn_wv, L1_attn_wo, L1_ffn_gate_w, L1_ffn_w_gate_up, L1_ffn_w_down, L1_ffn_shared_w_gate_up, L1_ffn_shared_w_down):

    def _L0_attn_ref(x, w_attn, w_proj, adapter_wte, gating):
        import jax, jax.numpy as jnp
        import numpy as np
        N_HEAD = 32
        ROPE_BASE = 10000.0

        def _rope_cos_sin(T, n_elem, dtype):
            theta = 1.0 / ROPE_BASE ** (jnp.arange(0, n_elem, 2, dtype=dtype) / n_elem)
            seq_idx = jnp.arange(T, dtype=dtype)
            idx_theta = jnp.outer(seq_idx, theta)
            idx_theta2 = jnp.concatenate([idx_theta, idx_theta], axis=-1)
            return (jnp.cos(idx_theta2), jnp.sin(idx_theta2))

        def _apply_rope(x, cos, sin):
            d2 = x.shape[-1] // 2
            rot = jnp.concatenate([-x[..., d2:], x[..., :d2]], axis=-1)
            return x * cos + rot * sin
        B, T, C = x.shape
        H = N_HEAD
        hd = C // H
        qkv = jnp.einsum('btc,oc->bto', x, w_attn)
        q, k, v = jnp.split(qkv, 3, axis=-1)
        q = q.reshape(B, T, H, hd).transpose(0, 2, 1, 3)
        k = k.reshape(B, T, H, hd).transpose(0, 2, 1, 3)
        v = v.reshape(B, T, H, hd).transpose(0, 2, 1, 3)
        cos, sin = _rope_cos_sin(T, hd, x.dtype)
        q = _apply_rope(q, cos, sin)
        k = _apply_rope(k, cos, sin)
        scores = jnp.einsum('bhqd,bhkd->bhqk', q, k) / jnp.sqrt(jnp.asarray(hd, x.dtype))
        causal = jnp.tril(jnp.ones((T, T), bool))
        scores = jnp.where(causal, scores, jnp.asarray(-jnp.inf, x.dtype))
        attn = jax.nn.softmax(scores, axis=-1)
        y = jnp.einsum('bhqk,bhkd->bhqd', attn, v)
        aT = adapter_wte.shape[0]
        prefix = adapter_wte[None]
        aqkv = jnp.einsum('btc,oc->bto', prefix, w_attn)
        _, ak, av = jnp.split(aqkv, 3, axis=-1)
        ak = ak.reshape(1, aT, H, hd).transpose(0, 2, 1, 3)
        av = av.reshape(1, aT, H, hd).transpose(0, 2, 1, 3)
        ascores = jnp.einsum('bhqd,xhkd->bhqk', q, ak) / jnp.sqrt(jnp.asarray(C, x.dtype))
        ascores = gating[0] * jax.nn.softmax(ascores.astype(jnp.float32), axis=-1).astype(q.dtype)
        y = y + jnp.einsum('bhqk,xhkd->bhqd', ascores, av)
        y = y.transpose(0, 2, 1, 3).reshape(B, T, C)
        return jnp.einsum('btc,oc->bto', y, w_proj)

    def _L0_ffn_ref(x, W, b, A, Bmat, LiMEs):
        import jax, jax.numpy as jnp
        import numpy as np
        NUM_EXPERTS = 8
        RANK = 32
        ALPHA = 16.0
        TOP_K = 2
        TEMPERATURE = 1.0
        GAMMA = 0.5
        SOFT_TOPK_TEMP = 0.5
        N_GRAM = 2
        EPS = 1e-06
        Bsz, T, d_in = x.shape
        E = LiMEs.shape[0]
        scaling = ALPHA / RANK
        H = jnp.einsum('btd,od->bto', x, W) + b
        z = jnp.einsum('btd,dr->btr', x, A)
        anchors = jnp.arange(N_GRAM - 1, T, N_GRAM)
        H_slice = H[:, anchors, :E]
        delta_slice = jnp.einsum('bar,er->bae', z[:, anchors], LiMEs)
        H_scale = jnp.maximum(jnp.max(jnp.abs(H_slice)), EPS)
        d_scale = jnp.maximum(jnp.max(jnp.abs(delta_slice)), EPS)
        logits = ((1.0 - GAMMA) * (H_slice / H_scale) + GAMMA * (delta_slice / d_scale)) / TEMPERATURE
        probs = jax.nn.softmax(logits, axis=-1)
        topk_vals, _ = jax.lax.top_k(probs, TOP_K)
        thresh = topk_vals[..., -1:]
        mask = jax.nn.sigmoid((probs - thresh) / SOFT_TOPK_TEMP)
        weights = probs * mask
        weights = weights / (jnp.sum(weights, axis=-1, keepdims=True) + 1e-09)
        weights_full = jnp.repeat(weights, N_GRAM, axis=1)
        p_mix = jnp.einsum('bte,er->btr', weights_full, LiMEs)
        delta = jnp.einsum('btr,ro->bto', z * p_mix, Bmat) * scaling
        return H + delta

    def _L1_attn_ref(x, wq, wk, wv, wo):
        import jax, jax.numpy as jnp
        import numpy as np
        DIM = 512
        N_HEADS = 32
        N_KV_HEADS = 8
        HEAD_DIM = 128
        B, S = (2, 256)
        b, s, _ = x.shape
        groups = N_HEADS // N_KV_HEADS
        q = (x @ wq.T).reshape(b, s, N_HEADS, HEAD_DIM).transpose(0, 2, 1, 3)
        k = (x @ wk.T).reshape(b, s, N_KV_HEADS, HEAD_DIM).transpose(0, 2, 1, 3)
        v = (x @ wv.T).reshape(b, s, N_KV_HEADS, HEAD_DIM).transpose(0, 2, 1, 3)
        qg = q.reshape(b, N_KV_HEADS, groups, s, HEAD_DIM)
        scores = jnp.einsum('bhgqd,bhkd->bhgqk', qg, k) * HEAD_DIM ** (-0.5)
        attn = jax.nn.softmax(scores, axis=-1)
        out = jnp.einsum('bhgqk,bhkd->bhgqd', attn, v)
        out = out.reshape(b, N_HEADS, s, HEAD_DIM).transpose(0, 2, 1, 3).reshape(b, s, N_HEADS * HEAD_DIM)
        return out @ wo.T

    def _L1_ffn_ref(hidden_states, gate_w, w_gate_up, w_down, shared_w_gate_up, shared_w_down):
        import jax, jax.numpy as jnp
        import numpy as np
        HIDDEN = 512
        MOE_INTER = 128
        SHARED_INTER = 512
        NUM_EXPERTS = 16
        TOP_K = 2

        def _moe_forward(x, gate_w, w_gate_up, w_down, shared_w_gate_up, shared_w_down):
            orig_shape = x.shape
            x2 = x.reshape(-1, orig_shape[-1])
            gu_s = x2 @ shared_w_gate_up.T
            g_s, u_s = jnp.split(gu_s, 2, axis=-1)
            shared_out = jax.nn.silu(g_s) * u_s @ shared_w_down.T
            logits = x2 @ gate_w.T
            probs = jax.nn.softmax(logits, axis=-1)
            topk_vals, topk_idx = jax.lax.top_k(probs, TOP_K)
            topk_vals = topk_vals / jnp.sum(topk_vals, axis=-1, keepdims=True)
            combine = jnp.sum(jax.nn.one_hot(topk_idx, NUM_EXPERTS, dtype=x2.dtype) * topk_vals[..., None], axis=1)
            gu = jnp.einsum('th,eih->eti', x2, w_gate_up)
            g, u = jnp.split(gu, 2, axis=-1)
            act = jax.nn.silu(g) * u
            out_e = jnp.einsum('eti,ehi->eth', act, w_down)
            moe_out = jnp.einsum('eth,te->th', out_e, combine)
            return (moe_out + shared_out).reshape(orig_shape)
        return _moe_forward(hidden_states, gate_w, w_gate_up, w_down, shared_w_gate_up, shared_w_down)
    x = L0_attn_x
    x = x + 0.5 * _L0_ffn_ref(_layernorm(x, axis=-1), L0_ffn_W, L0_ffn_b, L0_ffn_A, L0_ffn_Bmat, L0_ffn_LiMEs)
    x = x + _L0_attn_ref(_layernorm(x, axis=-1), L0_attn_w_attn, L0_attn_w_proj, L0_attn_adapter_wte, L0_attn_gating)
    x = x + 0.5 * _L0_ffn_ref(_layernorm(x, axis=-1), L0_ffn_W, L0_ffn_b, L0_ffn_A, L0_ffn_Bmat, L0_ffn_LiMEs)
    x = x + 0.5 * _L1_ffn_ref(_layernorm(x, axis=-1), L1_ffn_gate_w, L1_ffn_w_gate_up, L1_ffn_w_down, L1_ffn_shared_w_gate_up, L1_ffn_shared_w_down)
    x = x + _L1_attn_ref(_layernorm(x, axis=-1), L1_attn_wq, L1_attn_wk, L1_attn_wv, L1_attn_wo)
    x = x + 0.5 * _L1_ffn_ref(_layernorm(x, axis=-1), L1_ffn_gate_w, L1_ffn_w_gate_up, L1_ffn_w_down, L1_ffn_shared_w_gate_up, L1_ffn_shared_w_down)
    return x

_drawn_inputs = setup_inputs


def setup_inputs(seed=0):
    import zlib

    import numpy as np

    out = dict(_drawn_inputs(seed))
    spreads = {}
    factors = {'L0_ffn_b': 7.151,
     'L0_ffn_A': 8.0,
     'L0_ffn_Bmat': 8.0,
     'L0_ffn_LiMEs': 8.0,
     'L1_attn_wq': 8.0,
     'L1_attn_wk': 8.0,
     'L1_ffn_gate_w': 5.575,
     'L1_ffn_w_gate_up': 5.204,
     'L1_ffn_w_down': 5.19}
    for name, (base, spread) in spreads.items():
        noise = np.random.default_rng([zlib.crc32(name.encode()), seed]).standard_normal(out[name].shape)
        drawn = base * np.exp(spread * noise) if base else spread * noise
        out[name] = jnp.asarray(drawn.astype(out[name].dtype))
    for name, factor in factors.items():
        out[name] = (out[name] * factor).astype(out[name].dtype)
    return out
```

```python
from contextlib import ExitStack

import numpy as np
import concourse.bass as bass
from concourse import mybir

F32 = mybir.dt.float32
F32R = mybir.dt.float32r
BF16 = mybir.dt.bfloat16
U32 = mybir.dt.uint32
ALU = mybir.AluOpType
ACT = mybir.ActivationFunctionType
AX = mybir.AxisListType.X
RMAX = bass.bass_isa.ReduceOp.max

P = 128
B, T, C = 2, 512, 512
NT = B * T // P
TB = T // P
KC = C // P
H0, HD0, AK = 32, 16, 10
GH = P // HD0
NG0 = H0 // GH
PAIRS = GH // 2
E0, RANK = 8, 32
NW0 = C + RANK + E0
HALF0 = NW0 // 2
H1, KV1, D1 = 32, 8, 128
G1 = H1 // KV1
E1, MI, SI = 16, 128, 512
UNITS = E1 + SI // MI
TRI = TB * (TB + 1) // 2


class Stage:

    used = []

    def __init__(self, nc, ctx, name):
        self.nc, self.ctx, self.name = nc, ctx, name

    @classmethod
    def recycle(cls, nc):
        nc.clear_and_free_semaphores(cls.used)
        cls.used = []
        nc.all_engine_barrier()

    def sb(self, name, shape, dt=F32):
        return self.ctx.enter_context(self.nc.sbuf_tensor(f"{self.name}_{name}", shape, dt))

    def ps(self, name, shape, dt=F32):
        return self.ctx.enter_context(self.nc.psum_tensor(f"{self.name}_{name}", shape, dt))

    def sem(self, name):
        Stage.used.append(self.nc.alloc_semaphore(f"{self.name}_{name}"))
        return Stage.used[-1]


def wait(eng, sem, count):
    if not (isinstance(count, int) and count <= 0):
        eng.wait_ge(sem, count)


def peeled(eng, n, body):
    body(0)
    with eng.Fori(1, n - 1) as i:
        body(i)
    body(n - 1)


def three_passes(pe, out, w_hi, w_lo, m_hi, m_lo, first, last):
    pe.matmul(out, w_hi, m_hi, start=first, stop=False)
    pe.matmul(out, w_hi, m_lo, start=False, stop=False)
    return pe.matmul(out, w_lo, m_hi, start=False, stop=last)


def spread(ap, shape):
    return ap.unsqueeze(len(shape) - 1).broadcast_to(shape)


def load_stage(nc, env, dram):
    with ExitStack() as ctx:
        s = Stage(nc, ctx, "load")
        loaded = s.sem("loaded")
        with nc.Block() as block:

            @block.sync
            def _(sp):
                sp.dma_start(env["ident"][:, :], dram["ident"]).then_inc(loaded, 16)
                sp.dma_start(env["x"][:, :, :], dram["x"].rearrange("(t p) c -> p t c", p=P)).then_inc(loaded, 16)
                sp.wait_ge(loaded, 32)


def layernorm_stage(nc, env, name):
    x, xhi, xlo, ident = env["x"], env["xhi"], env["xlo"], env["ident"]
    with ExitStack() as ctx:
        s = Stage(nc, ctx, name)
        stats, mv = s.sb("stats", [P, NT, 6]), s.sb("mv", [P, NT, 2])
        ve, sd = s.sb("ve", [P, NT]), s.sb("sd", [P, NT])
        ra, rb, rc = s.sb("ra", [P, NT]), s.sb("rb", [P, NT]), s.sb("rc", [P, NT])
        xn = s.sb("xn", [P, NT, C])
        turned = [s.ps(f"turned{n}", [P, 512]) for n in range(8)]
        stats_ready, mv_ready, var_ready, std_ready = (s.sem(n) for n in ("stats_ready", "mv_ready", "var_ready", "std_ready"))
        rstd_step, xn_ready, turned_ready = (s.sem(n) for n in ("rstd_step", "xn_ready", "turned_ready"))
        hi_ready, lo_ready = s.sem("hi_ready"), s.sem("lo_ready")
        banks = [(h, k) for h in range(B) for k in range(KC)]

        with nc.Block() as block:

            @block.vector
            def _(dve):
                for t in range(NT):
                    dve.bn_stats(stats[:, t, :], x[:, t, :]).then_inc(stats_ready, 1)
                for t in range(NT):
                    dve.wait_ge(stats_ready, t + 1)
                    dve.bn_aggr(mv[:, t, :], stats[:, t, :]).then_inc(mv_ready, 1)
                dve.wait_ge(mv_ready, NT)
                dve.tensor_scalar(ve[:, :], mv[:, :, 1], 1e-5, None, ALU.add).then_inc(var_ready, 1)
                dve.wait_ge(std_ready, 1)
                dve.reciprocal(ra[:, :], sd[:, :]).then_inc(rstd_step, 1)
                dve.wait_ge(rstd_step, 1)
                dve.tensor_tensor(rb[:, :], ra[:, :], ra[:, :], ALU.mult).then_inc(rstd_step, 1)
                dve.wait_ge(rstd_step, 2)
                dve.tensor_tensor(rc[:, :], rb[:, :], ve[:, :], ALU.mult).then_inc(rstd_step, 1)
                dve.wait_ge(rstd_step, 3)
                dve.tensor_scalar(rb[:, :], rc[:, :], -0.5, 1.5, ALU.mult, ALU.add).then_inc(rstd_step, 1)
                dve.wait_ge(rstd_step, 4)
                dve.tensor_tensor(rc[:, :], ra[:, :], rb[:, :], ALU.mult).then_inc(rstd_step, 1)
                dve.wait_ge(rstd_step, 5)
                for t in range(NT):
                    dve.tensor_scalar(xn[:, t, :], x[:, t, :], mv[:, t, 0:1], rc[:, t:t + 1],
                                      ALU.subtract, ALU.mult).then_inc(xn_ready, 1)
                for n, (h, k) in enumerate(banks):
                    dve.wait_ge(hi_ready, n + 1)
                    dve.tensor_tensor(xlo[:, k, h * T:(h + 1) * T], turned[n][:, :], xhi[:, k, h * T:(h + 1) * T],
                                      ALU.subtract).then_inc(lo_ready, 1)

            @block.scalar
            def _(act):
                act.wait_ge(var_ready, 1)
                act.activation(sd[:, :], ve[:, :], ACT.Sqrt).then_inc(std_ready, 1)
                for n, (h, k) in enumerate(banks):
                    act.wait_ge(turned_ready, n + 1)
                    act.activation(xhi[:, k, h * T:(h + 1) * T], turned[n][:, :], ACT.Copy).then_inc(hi_ready, 1)

            @block.tensor
            def _(pe):
                for n, (h, k) in enumerate(banks):
                    pe.wait_ge(xn_ready, TB * (h + 1))
                    for t in range(TB):
                        last = pe.transpose(turned[n][:, t * P:(t + 1) * P], xn[:, h * TB + t, k * P:(k + 1) * P],
                                            ident[:, :])
                    last.then_inc(turned_ready, 1)


def lime_ffn_stage(nc, env, dram, name):
    x, xhi, xlo, ident = env["x"], env["xhi"], env["xlo"], env["ident"]
    with ExitStack() as ctx:
        s = Stage(nc, ctx, name)
        w, whi, wlo = s.sb("w", [P, KC, NW0]), s.sb("whi", [P, KC, NW0], F32R), s.sb("wlo", [P, KC, NW0], F32R)
        a_t, l_t, lime, bmat = s.sb("a_t", [RANK, C]), s.sb("l_t", [RANK, E0]), s.sb("lime", [E0, RANK]), s.sb("bmat", [RANK, C])
        bias, pair, odd = s.sb("bias", [P, C]), s.sb("pair", [P, P]), s.sb("odd", [P, 2])
        z, dl, hs = s.sb("z", [P, NT, RANK]), s.sb("dl", [P, NT, E0]), s.sb("hs", [P, NT, E0])
        signed = s.sb("signed", [P, 4, NT * E0])
        peak, peaks, scale = s.sb("peak", [P, 4]), s.sb("peaks", [P, 4]), s.sb("scale", [P, 2])
        inv = s.sb("inv", [P, 2])
        lg, lh = s.sb("lg", [P, NT, E0]), s.sb("lh", [P, NT, E0])
        pr, mk, wt = s.sb("pr", [P, NT, E0]), s.sb("mk", [P, NT, E0]), s.sb("wt", [P, NT, E0])
        mk2, ex = s.sb("mk2", [P, NT, E0]), s.sb("ex", [P, NT, E0])
        r1, r2, r3, r4 = (s.sb(f"r{n}", [P, NT]) for n in range(4))
        top = s.sb("top", [P, NT, 8])
        wt_t, zp, zp_t = s.sb("wt_t", [E0, NT * P]), s.sb("zp", [P, NT, RANK]), s.sb("zp_t", [RANK, NT * P])
        bank = [s.ps(f"bank{n}", [P, 512]) for n in range(8)]
        w_loaded, c_loaded = s.sem("w_loaded"), s.sem("c_loaded")
        al_ready, al_copied, whi_ready, wlo_ready = (s.sem(n) for n in ("al_ready", "al_copied", "whi_ready", "wlo_ready"))
        h_ready, h_taken, bias_added, col_taken = (s.sem(n) for n in ("h_ready", "h_taken", "bias_added", "col_taken"))
        route, peak_ready, peaks_ready = s.sem("route"), s.sem("peak_ready"), s.sem("peaks_ready")
        logit_ready, exp_ready, gap_ready, sig_ready = (s.sem(n) for n in ("logit_ready", "exp_ready", "gap_ready", "sig_ready"))
        wt_ready, wtt_ready, wtt_copied, mix_ready = (s.sem(n) for n in ("wt_ready", "wtt_ready", "wtt_copied", "mix_ready"))
        zp_ready, zpt_ready, zpt_copied, delta_ready = (s.sem(n) for n in ("zp_ready", "zpt_ready", "zpt_copied", "delta_ready"))
        x_added = s.sem("x_added")
        n_const = 7

        with nc.Block() as block:

            @block.sync
            def _(sp):
                sp.dma_start(a_t[:, :], dram["a_t"]).then_inc(c_loaded, 16)
                sp.dma_start(l_t[:, :], dram["l_t"]).then_inc(c_loaded, 16)
                sp.dma_start(w[:, :, 0:C + RANK], dram["w0"]).then_inc(w_loaded, 16)
                for tile, src in ((bias, "bias"), (odd, "odd"), (pair, "pair"), (lime, "lime"), (bmat, "bmat")):
                    sp.dma_start(tile[:, :], dram[src]).then_inc(c_loaded, 16)
                sp.wait_ge(c_loaded, 16 * n_const)

            @block.tensor
            def _(pe):
                pe.wait_ge(c_loaded, 16 * n_const)
                for k in range(KC):
                    last = pe.matmul(bank[0][:, k * E0:(k + 1) * E0], a_t[:, k * P:(k + 1) * P], l_t[:, :],
                                     start=True, stop=True)
                last.then_inc(al_ready, 1)
                pe.wait_ge(al_copied, 1)
                pe.wait_ge(wlo_ready, 1)
                for t in range(NT):
                    if t >= 4:
                        pe.wait_ge(h_taken, t - 3)
                    for half in range(2):
                        out = bank[2 * (t % 4) + half][:, 0:HALF0]
                        cols = slice(half * HALF0, (half + 1) * HALF0)
                        for k in range(KC):
                            tok = slice(t * P, (t + 1) * P)
                            last = three_passes(pe, out, xhi[:, k, tok], xlo[:, k, tok], whi[:, k, cols], wlo[:, k, cols],
                                                k == 0, k == KC - 1)
                    last.then_inc(h_ready, 1)
                pe.wait_ge(wt_ready, 1)
                for t in range(NT):
                    last = pe.matmul(bank[t // 4][0:E0, t % 4 * P:(t % 4 + 1) * P], wt[:, t, :], pair[:, :],
                                     start=True, stop=True)
                last.then_inc(wtt_ready, 1)
                pe.wait_ge(wtt_copied, 2)
                for t in range(NT):
                    last = pe.matmul(bank[2][:, t * RANK:(t + 1) * RANK], wt_t[:, t * P:(t + 1) * P], lime[:, :],
                                     start=True, stop=True)
                last.then_inc(mix_ready, 1)
                pe.wait_ge(zp_ready, 1)
                for t in range(NT):
                    last = pe.transpose(bank[t // 4][0:RANK, t % 4 * P:(t % 4 + 1) * P], zp[:, t, :], ident[:, :])
                last.then_inc(zpt_ready, 1)
                pe.wait_ge(zpt_copied, 2)
                for t in range(NT):
                    if t >= 4:
                        pe.wait_ge(x_added, t - 3)
                    pe.matmul(bank[4 + t % 4][:, :], zp_t[:, t * P:(t + 1) * P], bmat[:, :],
                              start=True, stop=True).then_inc(delta_ready, 1)

            @block.scalar
            def _(act):
                act.wait_ge(w_loaded, 16)
                act.wait_ge(al_copied, 1)
                act.activation(whi[:, :, :], w[:, :, :], ACT.Copy).then_inc(whi_ready, 1)
                act.wait_ge(logit_ready, 1)
                act.activation(ex[:, :, :], lg[:, :, :], ACT.Exp).then_inc(exp_ready, 1)
                act.wait_ge(gap_ready, 1)
                act.activation(mk[:, :, :], lh[:, :, :], ACT.Exp, scale=-2.0).then_inc(sig_ready, 1)

            @block.gpsimd
            def _(pool):
                pool.wait_ge(peak_ready, 1)
                pool.partition_all_reduce(peaks[:, :], peak[:, :], P, RMAX).then_inc(peaks_ready, 1)

            @block.vector
            def _(dve):
                step = [0]

                def routed(ins):
                    step[0] += 1
                    ins.then_inc(route, 1)
                    dve.wait_ge(route, step[0])

                dve.wait_ge(al_ready, 1)
                dve.wait_ge(w_loaded, 16)
                dve.tensor_copy(w[:, :, C + RANK:NW0], bank[0][:, 0:KC * E0].rearrange("p (k e) -> p k e", k=KC)).then_inc(al_copied, 1)
                dve.wait_ge(whi_ready, 1)
                dve.tensor_tensor(wlo[:, :, :], w[:, :, :], whi[:, :, :], ALU.subtract).then_inc(wlo_ready, 1)
                dve.wait_ge(c_loaded, 16 * n_const)
                for t in range(NT):
                    dve.scalar_tensor_tensor(out=x[:, t, :], in0=bias[:, :], scalar=0.5, in1=x[:, t, :],
                                             op0=ALU.mult, op1=ALU.add).then_inc(bias_added, 1)
                for t in range(NT):
                    lo_bank, hi_bank = bank[2 * (t % 4)], bank[2 * (t % 4) + 1]
                    dve.wait_ge(h_ready, t + 1)
                    dve.wait_ge(bias_added, t + 1)
                    dve.tensor_tensor(hs[:, t, :], lo_bank[:, 0:E0], bias[:, 0:E0], ALU.add).then_inc(col_taken, 1)
                    dve.tensor_copy(z[:, t, :], hi_bank[:, C - HALF0:C - HALF0 + RANK]).then_inc(col_taken, 1)
                    dve.tensor_copy(dl[:, t, :], hi_bank[:, C - HALF0 + RANK:HALF0]).then_inc(col_taken, 1)
                    dve.scalar_tensor_tensor(out=x[:, t, 0:HALF0], in0=lo_bank[:, 0:HALF0], scalar=0.5,
                                             in1=x[:, t, 0:HALF0], op0=ALU.mult, op1=ALU.add).then_inc(col_taken, 1)
                    dve.scalar_tensor_tensor(out=x[:, t, HALF0:C], in0=hi_bank[:, 0:C - HALF0], scalar=0.5,
                                             in1=x[:, t, HALF0:C], op0=ALU.mult, op1=ALU.add).then_inc(h_taken, 1)
                dve.wait_ge(col_taken, 4 * NT)
                flat = lambda a: a[:, :, :].rearrange("p t e -> p (t e)")
                for n, src in enumerate((hs, hs, dl, dl)):
                    dve.tensor_scalar(signed[:, n, :], flat(src), odd[:, n % 2:n % 2 + 1], None, ALU.mult).then_inc(route, 1)
                step[0] += 4
                dve.wait_ge(route, step[0])
                dve.tensor_reduce(peak[:, :], signed[:, :, :], AX, ALU.max).then_inc(peak_ready, 1)
                dve.wait_ge(peaks_ready, 1)
                pk = peaks[:, :].rearrange("p (a b) -> p a b", b=2)
                routed(dve.tensor_tensor(scale[:, :], pk[:, :, 0], pk[:, :, 1], ALU.max))
                routed(dve.tensor_scalar(scale[:, :], scale[:, :], 1e-6, None, ALU.max))
                routed(dve.reciprocal(inv[:, :], scale[:, :]))
                routed(dve.tensor_scalar(inv[:, :], inv[:, :], 0.5, None, ALU.mult))
                routed(dve.tensor_scalar(lh[:, :, :], hs[:, :, :], inv[:, 0:1], None, ALU.mult))
                routed(dve.scalar_tensor_tensor(out=flat(lg), in0=flat(dl), scalar=inv[:, 1:2], in1=flat(lh),
                                                op0=ALU.mult, op1=ALU.add))
                routed(dve.tensor_reduce(r1[:, :], lg[:, :, :], AX, ALU.max))
                dve.tensor_tensor(lg[:, :, :], lg[:, :, :], spread(r1[:, :], [P, NT, E0]), ALU.subtract).then_inc(logit_ready, 1)
                dve.wait_ge(exp_ready, 1)
                routed(dve.tensor_reduce(r2[:, :], ex[:, :, :], AX, ALU.add))
                routed(dve.reciprocal(r3[:, :], r2[:, :]))
                routed(dve.tensor_tensor(pr[:, :, :], ex[:, :, :], spread(r3[:, :], [P, NT, E0]), ALU.mult))
                for t in range(NT):
                    dve.max(top[:, t, :], pr[:, t, :]).then_inc(route, 1)
                step[0] += NT
                dve.wait_ge(route, step[0])
                dve.tensor_tensor(lh[:, :, :], pr[:, :, :], spread(top[:, :, 1], [P, NT, E0]), ALU.subtract).then_inc(gap_ready, 1)
                dve.wait_ge(sig_ready, 1)
                routed(dve.tensor_scalar(mk[:, :, :], mk[:, :, :], 1.0, None, ALU.add))
                routed(dve.reciprocal(mk2[:, :, :], mk[:, :, :]))
                routed(dve.tensor_tensor(mk[:, :, :], pr[:, :, :], mk2[:, :, :], ALU.mult))
                routed(dve.tensor_reduce(r1[:, :], mk[:, :, :], AX, ALU.add))
                routed(dve.tensor_scalar(r2[:, :], r1[:, :], 1e-9, None, ALU.add))
                routed(dve.reciprocal(r4[:, :], r2[:, :]))
                dve.tensor_tensor(wt[:, :, :], mk[:, :, :], spread(r4[:, :], [P, NT, E0]), ALU.mult).then_inc(wt_ready, 1)
                dve.wait_ge(wtt_ready, 1)
                for n in range(2):
                    dve.tensor_copy(wt_t[:, n * 512:(n + 1) * 512], bank[n][0:E0, :]).then_inc(wtt_copied, 1)
                dve.wait_ge(mix_ready, 1)
                dve.scalar_tensor_tensor(out=flat(zp), in0=bank[2][:, 0:NT * RANK], scalar=0.25, in1=flat(z),
                                         op0=ALU.mult, op1=ALU.mult).then_inc(zp_ready, 1)
                dve.wait_ge(zpt_ready, 1)
                for n in range(2):
                    dve.tensor_copy(zp_t[:, n * 512:(n + 1) * 512], bank[n][0:RANK, :]).then_inc(zpt_copied, 1)
                dve.wait_ge(h_taken, NT)
                for t in range(NT):
                    dve.wait_ge(delta_ready, t + 1)
                    dve.tensor_tensor(x[:, t, :], bank[4 + t % 4][:, :], x[:, t, :], ALU.add).then_inc(x_added, 1)


def moe_stage(nc, env, dram, name):
    x, xhi, xlo, ident = env["x"], env["xhi"], env["xlo"], env["ident"]
    NC = KC * 2 * MI + C
    with ExitStack() as ctx:
        s = Stage(nc, ctx, name)
        comb = s.sb("comb", [P, NT, UNITS])
        router_stage(nc, env, dram, name + "r", comb)
        raw = [s.sb(f"raw{n}", [P, NC]) for n in range(2)]
        whi = [s.sb(f"whi{n}", [P, NC], F32R) for n in range(2)]
        wlo = [s.sb(f"wlo{n}", [P, NC], F32R) for n in range(2)]
        sil = [s.sb(f"sil{n}", [P, T]) for n in range(2)]
        prod = [s.sb(f"prod{n}", [P, T]) for n in range(2)]
        ahi = [s.sb(f"ahi{n}", [P, T], F32R) for n in range(2)]
        alo = [s.sb(f"alo{n}", [P, T], F32R) for n in range(2)]
        gate = [s.ps(f"gate{n}", [P, T]) for n in range(2)]
        up = [s.ps(f"up{n}", [P, T]) for n in range(2)]
        down = [s.ps(f"down{n}", [P, C]) for n in range(TB)]
        loaded = [s.sem(f"loaded{n}") for n in range(2)]
        whi_ready = [s.sem(f"whi_ready{n}") for n in range(2)]
        wlo_ready = [s.sem(f"wlo_ready{n}") for n in range(2)]
        gate_ready, up_ready, sil_ready = s.sem("gate_ready"), s.sem("up_ready"), s.sem("sil_ready")
        prod_ready = [s.sem(f"prod_ready{n}") for n in range(2)]
        ahi_ready, alo_ready, down_ready = s.sem("ahi_ready"), s.sem("alo_ready"), s.sem("down_ready")
        added = [s.sem(f"added{n}") for n in range(TB)]
        last_pair = UNITS // 2 - 1
        STEPS = [(0, 0), (0, 1), (1, 0), (1, 1)]

        def gu(w, k, part):
            return w[:, k * 2 * MI + part * MI:k * 2 * MI + (part + 1) * MI]

        def dn(w):
            return w[:, KC * 2 * MI:NC]

        with nc.Block() as block:

            @block.sync
            def _(sp):
                def load(slot, unit):
                    sp.dma_start(raw[slot][:, :], dram["moe_w"][unit]).then_inc(loaded[slot], 16)
                load(0, 0)
                load(1, 1)
                with sp.Fori(0, last_pair) as i:
                    for slot in range(2):
                        wait(sp, wlo_ready[slot], i + 1)
                        sp.dma_start(raw[slot][:, :], dram["moe_w"][bass.ds(2 * i + 2 + slot, 1), :, :].rearrange("a p n -> p (a n)")).then_inc(loaded[slot], 16)

            @block.tensor
            def _(pe):
                def body(i):
                    def gate_up(j):
                        slot, half = STEPS[j]
                        if half == 0:
                            wait(pe, whi_ready[slot], i + 1)
                            wait(pe, wlo_ready[slot], i + 1)
                        wait(pe, prod_ready[half], 2 * i + slot)
                        for part, out, ready in ((0, gate[half], gate_ready), (1, up[half], up_ready)):
                            for k in range(KC):
                                last = three_passes(pe, out[:, :], gu(whi[slot], k, part), gu(wlo[slot], k, part),
                                                    xhi[:, k, half * T:(half + 1) * T], xlo[:, k, half * T:(half + 1) * T],
                                                    k == 0, k == KC - 1)
                            last.then_inc(ready, 1)

                    def down_steps(j):
                        slot, half = STEPS[j]
                        wait(pe, ahi_ready, 4 * i + j + 1)
                        wait(pe, alo_ready, 4 * i + j + 1)
                        for t in range(TB):
                            tok = slice(t * P, (t + 1) * P)
                            wait(pe, added[t], 4 * i + j)
                            three_passes(pe, down[t][:, :], ahi[half][:, tok], alo[half][:, tok], dn(whi[slot]), dn(wlo[slot]),
                                         True, True).then_inc(down_ready, 1)

                    gate_up(0)
                    for j in range(1, 4):
                        gate_up(j)
                        down_steps(j - 1)
                    down_steps(3)

                peeled(pe, last_pair + 1, body)

            @block.scalar
            def _(act):
                def split_hi(slot, n, downs):
                    wait(act, loaded[slot], 16 * n + 16)
                    wait(act, down_ready, downs)
                    act.activation(whi[slot][:, :], raw[slot][:, :], ACT.Copy).then_inc(whi_ready[slot], 1)

                def body(i):
                    last = isinstance(i, int) and i == last_pair
                    for j, (slot, half) in enumerate(STEPS):
                        wait(act, gate_ready, 4 * i + j + 1)
                        wait(act, prod_ready[half], 2 * i + slot)
                        act.activation(sil[half][:, :], gate[half][:, :], ACT.Silu).then_inc(sil_ready, 1)
                        wait(act, prod_ready[half], 2 * i + slot + 1)
                        wait(act, down_ready, 16 * i + 4 * max(j - 1, 0))
                        act.activation(ahi[half][:, :], prod[half][:, :], ACT.Copy).then_inc(ahi_ready, 1)
                        if j == 0:
                            split_hi(1, i, 16 * i)
                        if j == 2 and not last:
                            split_hi(0, i + 1, 16 * i + 8)

                split_hi(0, 0, 0)
                peeled(act, last_pair + 1, body)

            @block.gpsimd
            def _(pool):
                def split_lo(slot, n):
                    wait(pool, whi_ready[slot], n + 1)
                    pool.tensor_tensor(wlo[slot][:, :], raw[slot][:, :], whi[slot][:, :], ALU.subtract).then_inc(wlo_ready[slot], 1)

                with pool.Fori(0, last_pair + 1) as i:
                    split_lo(0, i)
                    split_lo(1, i)

            @block.vector
            def _(dve):
                def body(i):
                    def add(j):
                        slot, half = STEPS[j]
                        for t in range(TB):
                            tile = half * TB + t
                            wait(dve, down_ready, 16 * i + 4 * j + t + 1)
                            wait(dve, added[t], 4 * i + j)
                            dve.scalar_tensor_tensor(out=x[:, tile, :], in0=down[t][:, :],
                                                     scalar=comb[:, tile, bass.ds(2 * i + slot, 1)], in1=x[:, tile, :],
                                                     op0=ALU.mult, op1=ALU.add).then_inc(added[t], 1)

                    for j, (slot, half) in enumerate(STEPS):
                        wait(dve, sil_ready, 4 * i + j + 1)
                        wait(dve, up_ready, 4 * i + j + 1)
                        wait(dve, alo_ready, 4 * i + max(j - 1, 0))
                        dve.tensor_tensor(prod[half][:, :], sil[half][:, :], up[half][:, :], ALU.mult).then_inc(prod_ready[half], 1)
                        wait(dve, ahi_ready, 4 * i + j + 1)
                        dve.tensor_tensor(alo[half][:, :], prod[half][:, :], ahi[half][:, :], ALU.subtract).then_inc(alo_ready, 1)
                        if j >= 1:
                            add(j - 1)
                    add(3)

                peeled(dve, last_pair + 1, body)


def router_stage(nc, env, dram, name, comb):
    xhi, xlo, ident = env["xhi"], env["xlo"], env["ident"]
    with ExitStack() as ctx:
        s = Stage(nc, ctx, name)
        gw = s.sb("gw", [P, KC, P])
        ghi, glo = s.sb("ghi", [P, KC, P], F32R), s.sb("glo", [P, KC, P], F32R)
        expert = s.sb("expert", [P, E1])
        lgt = s.sb("lgt", [E1, NT * P])
        lg, ex, pr = s.sb("lg", [P, NT, E1]), s.sb("ex", [P, NT, E1]), s.sb("pr", [P, NT, E1])
        one, two = s.sb("one", [P, NT, E1]), s.sb("two", [P, NT, E1])
        mx, sm, rs = s.sb("mx", [P, NT]), s.sb("sm", [P, NT]), s.sb("rs", [P, NT])
        top, at, atf = s.sb("top", [P, NT, 8]), s.sb("at", [P, NT, 8], U32), s.sb("atf", [P, NT, 8])
        wtop = s.sb("wtop", [P, NT, 2])
        lt = [s.ps(f"lt{n}", [P, 512]) for n in range(2)]
        lp = s.ps("lp", [P, NT, E1])
        loaded, zeroed, ghi_ready, glo_ready = (s.sem(n) for n in ("loaded", "zeroed", "ghi_ready", "glo_ready"))
        lt_ready, lt_copied, lp_ready = s.sem("lt_ready"), s.sem("lt_copied"), s.sem("lp_ready")
        route, logit_ready, exp_ready = s.sem("route"), s.sem("logit_ready"), s.sem("exp_ready")

        with nc.Block() as block:

            @block.sync
            def _(sp):
                sp.dma_start(expert[:, :], dram["expert"]).then_inc(loaded, 16)
                sp.wait_ge(zeroed, 1)
                sp.dma_start(gw[:, :, 0:E1], dram["gate_w"]).then_inc(loaded, 16)

            @block.tensor
            def _(pe):
                pe.wait_ge(ghi_ready, 1)
                pe.wait_ge(glo_ready, 1)
                for half in range(2):
                    tok = slice(half * T, (half + 1) * T)
                    for k in range(KC):
                        last = three_passes(pe, lt[half][:, :], ghi[:, k, :], glo[:, k, :], xhi[:, k, tok], xlo[:, k, tok],
                                            k == 0, k == KC - 1)
                    last.then_inc(lt_ready, 1)
                pe.wait_ge(lt_copied, 2)
                for t in range(NT):
                    last = pe.transpose(lp[:, t, :], lgt[:, t * P:(t + 1) * P], ident[0:E1, 0:E1])
                last.then_inc(lp_ready, 1)

            @block.scalar
            def _(act):
                act.wait_ge(loaded, 32)
                act.activation(ghi[:, :, :], gw[:, :, :], ACT.Copy).then_inc(ghi_ready, 1)
                act.wait_ge(logit_ready, 1)
                act.activation(ex[:, :, :], lg[:, :, :], ACT.Exp).then_inc(exp_ready, 1)

            @block.vector
            def _(dve):
                step = [0]

                def routed(ins):
                    step[0] += 1
                    ins.then_inc(route, 1)
                    dve.wait_ge(route, step[0])

                dve.memset(gw[:, :, :], 0.0).then_inc(zeroed, 1)
                routed(dve.memset(comb[:, :, :], 0.5))
                dve.wait_ge(ghi_ready, 1)
                dve.tensor_tensor(glo[:, :, :], gw[:, :, :], ghi[:, :, :], ALU.subtract).then_inc(glo_ready, 1)
                for half in range(2):
                    dve.wait_ge(lt_ready, half + 1)
                    dve.tensor_copy(lgt[:, half * T:(half + 1) * T], lt[half][0:E1, :]).then_inc(lt_copied, 1)
                dve.wait_ge(lp_ready, 1)
                routed(dve.tensor_reduce(mx[:, :], lp[:, :, :], AX, ALU.max))
                dve.tensor_tensor(lg[:, :, :], lp[:, :, :], spread(mx[:, :], [P, NT, E1]), ALU.subtract).then_inc(logit_ready, 1)
                dve.wait_ge(exp_ready, 1)
                routed(dve.tensor_reduce(sm[:, :], ex[:, :, :], AX, ALU.add))
                routed(dve.reciprocal(rs[:, :], sm[:, :]))
                routed(dve.tensor_tensor(pr[:, :, :], ex[:, :, :], spread(rs[:, :], [P, NT, E1]), ALU.mult))
                for t in range(NT):
                    dve.max(top[:, t, :], pr[:, t, :]).then_inc(route, 1)
                step[0] += NT
                dve.wait_ge(route, step[0])
                for t in range(NT):
                    dve.max_index(at[:, t, :], top[:, t, :], pr[:, t, :]).then_inc(route, 1)
                step[0] += NT
                dve.wait_ge(route, step[0])
                routed(dve.tensor_copy(atf[:, :, :], at[:, :, :]))
                routed(dve.tensor_tensor(mx[:, :], top[:, :, 0], top[:, :, 1], ALU.add))
                routed(dve.reciprocal(sm[:, :], mx[:, :]))
                routed(dve.tensor_scalar(rs[:, :], sm[:, :], 0.5, None, ALU.mult))
                routed(dve.tensor_tensor(wtop[:, :, :], top[:, :, 0:2], spread(rs[:, :], [P, NT, 2]), ALU.mult))
                for n, out in enumerate((one, two)):
                    routed(dve.tensor_tensor(ex[:, :, :], expert[:, :].unsqueeze(1).broadcast_to([P, NT, E1]),
                                             spread(atf[:, :, n], [P, NT, E1]), ALU.is_equal))
                    routed(dve.tensor_tensor(out[:, :, :], ex[:, :, :], spread(wtop[:, :, n], [P, NT, E1]), ALU.mult))
                routed(dve.tensor_tensor(comb[:, :, 0:E1], one[:, :, :], two[:, :, :], ALU.add))


def gqa_stage(nc, env, dram, name):
    x, xhi, xlo, ident = env["x"], env["xhi"], env["xlo"], env["ident"]
    SCALE = float(D1) ** -0.5
    NU = B * G1
    with ExitStack() as ctx:
        s = Stage(nc, ctx, name)
        parts = {"kv": KC * 2 * D1, "q": G1 * KC * D1, "o": G1 * C}
        raw = {k: s.sb(f"{k}raw", [P, n]) for k, n in parts.items()}
        whi = {k: s.sb(f"{k}whi", [P, n], F32R) for k, n in parts.items()}
        wlo = {k: s.sb(f"{k}wlo", [P, n], F32R) for k, n in parts.items()}
        khi, klo = s.sb("khi", [P, B * T], F32R), s.sb("klo", [P, B * T], F32R)
        vt = s.sb("vt", [P, B * T])
        vhi, vlo = s.sb("vhi", [P, NT * D1], F32R), s.sb("vlo", [P, NT * D1], F32R)
        qhi = [s.sb(f"qhi{n}", [P, T], F32R) for n in range(2)]
        qlo = [s.sb(f"qlo{n}", [P, T], F32R) for n in range(2)]
        prob = [s.sb(f"prob{n}", [P, TB, T]) for n in range(2)]
        nmax, rsum, rinv = s.sb("nmax", [P, 2 * TB]), s.sb("rsum", [P, 2 * TB]), s.sb("rinv", [P, 2 * TB])
        pthi, ptlo = s.sb("pthi", [P, TB, T], F32R), s.sb("ptlo", [P, TB, T], F32R)
        ohi, olo = s.sb("ohi", [P, NU, T], F32R), s.sb("olo", [P, NU, T], F32R)
        work = [s.ps(f"work{n}", [P, 512]) for n in range(2)]
        score = [s.ps(f"score{n}", [P, T]) for n in range(2)]
        turned = [s.ps(f"turned{n}", [P, 512]) for n in range(2)]
        outp = [s.ps(f"outp{n}", [P, T]) for n in range(2)]
        loaded = {k: s.sem(f"{k}_loaded") for k in parts}
        whi_ready = {k: s.sem(f"{k}whi_ready") for k in parts}
        wlo_ready = {k: s.sem(f"{k}wlo_ready") for k in parts}
        work_ready = [s.sem(f"work_ready{n}") for n in range(2)]
        work_free = [s.sem(f"work_free{n}") for n in range(2)]
        work_hi = [s.sem(f"work_hi{n}") for n in range(2)]
        score_ready, nmax_ready, exp_ready = s.sem("score_ready"), s.sem("nmax_ready"), s.sem("exp_ready")
        rinv_ready, norm_ready, turned_ready = s.sem("rinv_ready"), s.sem("norm_ready"), s.sem("turned_ready")
        pthi_ready, ptlo_ready, out_ready = s.sem("pthi_ready"), s.sem("ptlo_ready"), s.sem("out_ready")
        ohi_ready, olo_ready = s.sem("ohi_ready"), s.sem("olo_ready")
        K_USE, V_USE, VT_USE, Q_USE, O_USE, USES = 0, 1, 2, 3, 3 + NU // 2, 3 + NU // 2 + TB
        HIS = 2 + NU // 2
        QT = 4 * NU
        LAST = KV1 - 1

        def col(a, n, w=P):
            return a[:, n * w:(n + 1) * w]

        with nc.Block() as block:

            @block.sync
            def _(sp):
                for k in ("kv", "q", "o"):
                    sp.dma_start(raw[k][:, :], dram["gqa_" + k][0]).then_inc(loaded[k], 16)
                with sp.Fori(0, LAST) as g:
                    for k, pieces in (("kv", 1), ("q", 1), ("o", 2)):
                        wait(sp, wlo_ready[k], pieces * (g + 1))
                        sp.dma_start(raw[k][:, :], dram["gqa_" + k][bass.ds(g + 1, 1), :, :].rearrange("a p n -> p (a n)")).then_inc(loaded[k], 16)

            @block.tensor
            def _(pe):
                def body(g):
                    def claim(bank, use):
                        wait(pe, work_free[bank], USES * g + use)

                    def project(bank, use, w, m):
                        claim(bank, use)
                        for k in range(KC):
                            hi, lo = w(whi, k), w(wlo, k)
                            last = three_passes(pe, work[bank][:, :], hi, lo, xhi[:, k, m], xlo[:, k, m], k == 0, k == KC - 1)
                        last.then_inc(work_ready[bank], 1)

                    def q_unit(u):
                        b, head = divmod(u, G1)
                        project(u % 2, Q_USE + u // 2, lambda w, k: col(w["q"], head * KC + k), slice(b * T, (b + 1) * T))

                    def scores(u, t):
                        b, n = u // G1, 4 * u + t
                        if t == 0:
                            wait(pe, work_free[u % 2], USES * g + Q_USE + u // 2 + 1)
                        wait(pe, exp_ready, QT * g + max(n - 1, 0))
                        three_passes(pe, score[t % 2][:, :], col(qhi[u % 2], t), col(qlo[u % 2], t),
                                     khi[:, b * T:(b + 1) * T], klo[:, b * T:(b + 1) * T], True, True).then_inc(score_ready, 1)

                    def turn(u, t):
                        n = 4 * u + t
                        wait(pe, norm_ready, QT * g + n + 1)
                        wait(pe, ptlo_ready, QT * g + max(n - 1, 0))
                        for k in range(TB):
                            last = pe.transpose(col(turned[t % 2], k), prob[u % 2][:, t, k * P:(k + 1) * P], ident[:, :])
                        last.then_inc(turned_ready, 1)

                    def values(u):
                        b = u // G1
                        wait(pe, pthi_ready, QT * g + 4 * u + 4)
                        wait(pe, ptlo_ready, QT * g + 4 * u + 4)
                        wait(pe, olo_ready, NU * g + max(u - 1, 0))
                        for k in range(TB):
                            last = three_passes(pe, outp[u % 2][:, :], col(vhi, b * TB + k), col(vlo, b * TB + k),
                                                pthi[:, k, :], ptlo[:, k, :], k == 0, k == TB - 1)
                        last.then_inc(out_ready, 1)

                    def out_projection(b):
                        wait(pe, ohi_ready, NU * g + G1 * (b + 1))
                        wait(pe, olo_ready, NU * g + G1 * (b + 1))
                        wait(pe, wlo_ready["o"], 2 * g + 2)
                        for t in range(TB):
                            bank, use = t % 2, O_USE + (b * TB + t) // 2
                            claim(bank, use)
                            for head in range(G1):
                                u, tok = b * G1 + head, slice(t * P, (t + 1) * P)
                                last = three_passes(pe, work[bank][:, :], ohi[:, u, tok], olo[:, u, tok], col(whi["o"], head, C),
                                                    col(wlo["o"], head, C), head == 0, head == G1 - 1)
                            last.then_inc(work_ready[bank], 1)

                    wait(pe, wlo_ready["kv"], g + 1)
                    for half in range(2):
                        project(half, K_USE, lambda w, k: col(w["kv"], 2 * k), slice(half * T, (half + 1) * T))
                    for half in range(2):
                        project(half, V_USE, lambda w, k: col(w["kv"], 2 * k + 1), slice(half * T, (half + 1) * T))
                    for half in range(2):
                        claim(half, VT_USE)
                        for t in range(TB):
                            last = pe.transpose(col(work[half], t), col(vt, half * TB + t), ident[:, :])
                        last.then_inc(work_ready[half], 1)
                    wait(pe, wlo_ready["q"], g + 1)
                    q_unit(0)
                    for u in range(NU):
                        for t in range(TB):
                            scores(u, t)
                            if u >= 1:
                                turn(u - 1, t)
                        if u + 1 < NU:
                            q_unit(u + 1)
                        if u >= 1:
                            values(u - 1)
                    out_projection(0)
                    for t in range(TB):
                        turn(NU - 1, t)
                    values(NU - 1)
                    out_projection(1)

                peeled(pe, KV1, body)

            @block.scalar
            def _(act):
                def split_hi(k, n):
                    wait(act, loaded[k], 16 * n + 16)
                    act.activation(whi[k][:, :], raw[k][:, :], ACT.Copy).then_inc(whi_ready[k], 1)

                def body(g):
                    last = isinstance(g, int) and g == LAST

                    def work_split(bank, use, out, scale=1.0):
                        wait(act, work_ready[bank], USES * g + use + 1)
                        act.activation(out, work[bank][:, :], ACT.Copy, scale=scale).then_inc(work_hi[bank], 1)

                    def q_split(u):
                        work_split(u % 2, Q_USE + u // 2, qhi[u % 2][:, :], SCALE)

                    def out_split(u):
                        wait(act, out_ready, NU * g + u + 1)
                        act.activation(ohi[:, u, :], outp[u % 2][:, :], ACT.Copy).then_inc(ohi_ready, 1)

                    def turned_split(u, t):
                        wait(act, turned_ready, QT * g + 4 * u + t + 1)
                        act.activation(pthi[:, :, t * P:(t + 1) * P], turned[t % 2][:, :].rearrange("p (k q) -> p k q", k=TB),
                                       ACT.Copy).then_inc(pthi_ready, 1)

                    for half in range(2):
                        work_split(half, K_USE, col(khi, half, T))
                    for half in range(2):
                        wait(act, work_ready[half], USES * g + V_USE + 1)
                        act.activation(col(vt, half, T), work[half][:, :], ACT.Copy).then_inc(work_free[half], 1)
                    for half in range(2):
                        work_split(half, VT_USE, col(vhi, half, T))
                    q_split(0)
                    for u in range(NU):
                        for t in range(TB):
                            n, slot = 4 * u + t, u % 2 * TB + t
                            wait(act, nmax_ready, QT * g + n + 1)
                            act.activation(prob[u % 2][:, t, :], score[t % 2][:, :], ACT.Exp, bias=nmax[:, slot:slot + 1],
                                           accum_out=rsum[:, slot:slot + 1]).then_inc(exp_ready, 1)
                            if u >= 1:
                                turned_split(u - 1, t)
                        if u + 1 < NU:
                            q_split(u + 1)
                        if u >= 1:
                            out_split(u - 1)
                        if u == 1:
                            split_hi("o", g)
                        if u == 4 and not last:
                            split_hi("kv", g + 1)
                        if u == NU - 1 and not last:
                            split_hi("q", g + 1)
                    for t in range(TB):
                        turned_split(NU - 1, t)
                    out_split(NU - 1)

                split_hi("kv", 0)
                split_hi("q", 0)
                peeled(act, KV1, body)

            @block.gpsimd
            def _(pool):
                def split_lo(k, n, piece=0, pieces=1):
                    wait(pool, whi_ready[k], n + 1)
                    w = parts[k] // pieces
                    pool.tensor_tensor(col(wlo[k], piece, w), col(raw[k], piece, w), col(whi[k], piece, w),
                                       ALU.subtract).then_inc(wlo_ready[k], 1)

                def body(g):
                    last = isinstance(g, int) and g == LAST

                    for u in range(NU):
                        for t in range(TB):
                            slot = u % 2 * TB + t
                            wait(pool, rinv_ready, QT * g + 4 * u + t + 1)
                            pool.tensor_tensor(prob[u % 2][:, t, :], prob[u % 2][:, t, :],
                                               rinv[:, slot:slot + 1].broadcast_to([P, T]), ALU.mult).then_inc(norm_ready, 1)
                        if u in (1, 3):
                            split_lo("o", g, u // 2, 2)
                        if u == 4 and not last:
                            split_lo("kv", g + 1)
                        if u == NU - 1 and not last:
                            split_lo("q", g + 1)

                split_lo("kv", 0)
                split_lo("q", 0)
                peeled(pool, KV1, body)

            @block.vector
            def _(dve):
                def body(g):
                    def work_split(bank, his, hi, lo):
                        wait(dve, work_hi[bank], HIS * g + his + 1)
                        dve.tensor_tensor(lo, work[bank][:, :], hi, ALU.subtract).then_inc(work_free[bank], 1)

                    def q_split(u):
                        bank = u % 2
                        wait(dve, work_hi[bank], HIS * g + 2 + u // 2 + 1)
                        dve.scalar_tensor_tensor(out=qlo[bank][:, :], in0=work[bank][:, :], scalar=SCALE, in1=qhi[bank][:, :],
                                                 op0=ALU.mult, op1=ALU.subtract).then_inc(work_free[bank], 1)

                    def turned_split(u, t):
                        wait(dve, pthi_ready, QT * g + 4 * u + t + 1)
                        dve.tensor_tensor(ptlo[:, :, t * P:(t + 1) * P], turned[t % 2][:, :].rearrange("p (k q) -> p k q", k=TB),
                                          pthi[:, :, t * P:(t + 1) * P], ALU.subtract).then_inc(ptlo_ready, 1)

                    def out_split(u):
                        wait(dve, ohi_ready, NU * g + u + 1)
                        dve.tensor_tensor(olo[:, u, :], outp[u % 2][:, :], ohi[:, u, :], ALU.subtract).then_inc(olo_ready, 1)

                    def add(b):
                        for t in range(TB):
                            tile, bank, use = b * TB + t, t % 2, O_USE + (b * TB + t) // 2
                            wait(dve, work_ready[bank], USES * g + use + 1)
                            dve.tensor_tensor(x[:, tile, :], work[bank][:, :], x[:, tile, :], ALU.add).then_inc(work_free[bank], 1)

                    for half in range(2):
                        work_split(half, 0, col(khi, half, T), col(klo, half, T))
                    for half in range(2):
                        work_split(half, 1, col(vhi, half, T), col(vlo, half, T))
                    q_split(0)
                    for u in range(NU):
                        for t in range(TB):
                            n, slot = 4 * u + t, u % 2 * TB + t
                            wait(dve, score_ready, QT * g + n + 1)
                            dve.tensor_reduce(nmax[:, slot:slot + 1], score[t % 2][:, :], AX, ALU.max, negate=True).then_inc(nmax_ready, 1)
                            if u >= 1:
                                turned_split(u - 1, t)
                            wait(dve, exp_ready, QT * g + n + 1)
                            dve.reciprocal(rinv[:, slot:slot + 1], rsum[:, slot:slot + 1]).then_inc(rinv_ready, 1)
                        if u + 1 < NU:
                            q_split(u + 1)
                        if u >= 1:
                            out_split(u - 1)
                    add(0)
                    for t in range(TB):
                        turned_split(NU - 1, t)
                    out_split(NU - 1)
                    add(1)

                peeled(dve, KV1, body)


def adapter_attention_stage(nc, env, dram, name):
    with ExitStack() as ctx:
        s = Stage(nc, ctx, name)
        q, k, v = (s.sb(n, [P, NG0 * B, TB, P]) for n in "qkv")
        ak, av = s.sb("ak", [GH * AK, NG0, P]), s.sb("av", [GH * AK, NG0, P])
        qkv_block(nc, env, dram, name + "a", q, k, v, ak, av)
        heads_block(nc, env, dram, name + "b", q, k, v, ak, av)
    projection_block(nc, env, dram, name + "c")


def qkv_block(nc, env, dram, name, q, k, v, ak, av):
    xhi, xlo = env["xhi"], env["xlo"]
    with ExitStack() as ctx:
        s = Stage(nc, ctx, name)
        raw = [s.sb(f"raw{n}", [P, KC, C]) for n in range(2)]
        whi = [s.sb(f"whi{n}", [P, KC, C], F32R) for n in range(2)]
        wlo = [s.sb(f"wlo{n}", [P, KC, C], F32R) for n in range(2)]
        pre, pre_hi, pre_lo = s.sb("pre", [P, KC, GH * AK]), s.sb("pre_hi", [P, KC, GH * AK], F32R), s.sb("pre_lo", [P, KC, GH * AK], F32R)
        rope = s.sb("rope", [P, 4, TB, HD0])
        tc = [s.sb(f"tc{n}", [P, H0, HD0]) for n in range(2)]
        ts = [s.sb(f"ts{n}", [P, H0, HD0]) for n in range(2)]
        rot = [s.ps(f"rot{n}", [P, C]) for n in range(4)]
        plain = [s.ps(f"plain{n}", [P, C]) for n in range(2)]
        loaded, pre_loaded = [s.sem(f"loaded{n}") for n in range(3)], s.sem("pre_loaded")
        whi_ready, wlo_ready, pre_hi_ready, pre_lo_ready = (s.sem(n) for n in ("whi_ready", "wlo_ready", "pre_hi_ready", "pre_lo_ready"))
        rot_ready, turned, summed = s.sem("rot_ready"), s.sem("turned"), s.sem("summed")
        plain_ready, plain_taken = s.sem("plain_ready"), s.sem("plain_taken")
        half = HD0 // 2

        def place(dst, t):
            b, tt = divmod(t, TB)
            return dst[:, b::B, tt, :]

        with nc.Block() as block:

            @block.sync
            def _(sp):
                for c in range(2):
                    sp.dma_start(raw[c][:, :, :], dram["w_attn"][:, :, c * C:(c + 1) * C]).then_inc(loaded[c], 16)
                sp.dma_start(rope[:, :, :, :], dram["rope"]).then_inc(pre_loaded, 16)
                sp.dma_start(pre[:, :, :], dram["prefix"]).then_inc(pre_loaded, 16)
                sp.wait_ge(wlo_ready, 1)
                sp.dma_start(raw[0][:, :, :], dram["w_attn"][:, :, 2 * C:3 * C]).then_inc(loaded[2], 16)

            @block.tensor
            def _(pe):
                rots = plains = 0
                for c in range(3):
                    w = c % 2
                    pe.wait_ge(wlo_ready, c + 1)
                    if c == 1:
                        pe.wait_ge(pre_lo_ready, 1)
                    for t in range(NT + (c > 0)):
                        adapter = t == NT
                        if adapter:
                            stat = lambda kc: (pre_hi[:, kc, :], pre_lo[:, kc, :])
                        else:
                            stat = lambda kc: (xhi[:, kc, t * P:(t + 1) * P], xlo[:, kc, t * P:(t + 1) * P])
                        if c < 2 and not adapter:
                            out, ready = rot[rots % 4][:, :], rot_ready
                            if rots >= 4:
                                pe.wait_ge(turned, 3 * (rots - 3))
                            rots += 1
                        else:
                            out, ready = plain[plains % 2], plain_ready
                            out = out[0:GH * AK, :] if adapter else out[:, :]
                            if plains >= 2:
                                pe.wait_ge(plain_taken, plains - 1)
                            plains += 1
                        for kc in range(KC):
                            hi, lo = stat(kc)
                            last = three_passes(pe, out, hi, lo, whi[w][:, kc, :], wlo[w][:, kc, :], kc == 0, kc == KC - 1)
                        last.then_inc(ready, 1)

            @block.scalar
            def _(act):
                def split(c, wait):
                    act.wait_ge(loaded[c], 16)
                    wait()
                    act.activation(whi[c % 2][:, :, :], raw[c % 2][:, :, :], ACT.Copy).then_inc(whi_ready, 1)

                split(0, lambda: None)
                split(1, lambda: None)
                act.wait_ge(pre_loaded, 32)
                act.activation(pre_hi[:, :, :], pre[:, :, :], ACT.Copy).then_inc(pre_hi_ready, 1)
                split(2, lambda: act.wait_ge(rot_ready, NT))
                act.wait_ge(plain_ready, 1)
                act.activation(ak[:, :, :], plain[0][0:GH * AK, :].rearrange("p (g f) -> p g f", f=P), ACT.Copy).then_inc(plain_taken, 1)
                for t in range(NT):
                    act.wait_ge(plain_ready, t + 2)
                    act.activation(place(v, t), plain[(t + 1) % 2][:, :].rearrange("p (g f) -> p g f", f=P), ACT.Copy).then_inc(plain_taken, 1)
                act.wait_ge(plain_ready, NT + 2)
                act.activation(av[:, :, :], plain[(NT + 1) % 2][0:GH * AK, :].rearrange("p (g f) -> p g f", f=P), ACT.Copy)

            @block.gpsimd
            def _(pool):
                for n in range(2 * NT):
                    dst, t = (q, k)[n // NT], n % NT
                    pool.wait_ge(turned, 3 * (n + 1))
                    pool.tensor_tensor(place(dst, t), tc[n % 2][:, :, :].rearrange("p (g h) d -> p g (h d)", g=NG0),
                                       ts[n % 2][:, :, :].rearrange("p (g h) d -> p g (h d)", g=NG0), ALU.add).then_inc(summed, 1)

            @block.vector
            def _(dve):
                def split(c):
                    dve.wait_ge(whi_ready, c + 1)
                    dve.tensor_tensor(wlo[c % 2][:, :, :], raw[c % 2][:, :, :], whi[c % 2][:, :, :], ALU.subtract).then_inc(wlo_ready, 1)

                split(0)
                split(1)
                dve.wait_ge(pre_hi_ready, 1)
                dve.tensor_tensor(pre_lo[:, :, :], pre[:, :, :], pre_hi[:, :, :], ALU.subtract).then_inc(pre_lo_ready, 1)
                for n in range(2 * NT):
                    c, t = divmod(n, NT)
                    tt, bank = t % TB, rot[n % 4][:, :].rearrange("p (h d) -> p h d", d=HD0)
                    if n == NT:
                        split(2)
                    cos = rope[:, 2 * c, tt, :].unsqueeze(1).broadcast_to([P, H0, HD0])
                    sin = rope[:, 2 * c + 1, tt, :].unsqueeze(1).broadcast_to([P, H0, HD0])
                    dve.wait_ge(rot_ready, n + 1)
                    if n >= 2:
                        dve.wait_ge(summed, n - 1)
                    dve.tensor_tensor(tc[n % 2][:, :, :], bank, cos, ALU.mult).then_inc(turned, 1)
                    dve.tensor_tensor(ts[n % 2][:, :, 0:half], bank[:, :, half:HD0], sin[:, :, 0:half], ALU.mult).then_inc(turned, 1)
                    dve.tensor_tensor(ts[n % 2][:, :, half:HD0], bank[:, :, 0:half], sin[:, :, half:HD0], ALU.mult).then_inc(turned, 1)


def heads_block(nc, env, dram, name, q, k, v, ak, av):
    xhi, xlo, ident = env["xhi"], env["xlo"], env["ident"]
    SLOT = (GH + 1) * HD0
    starts = [P * (t * (t + 1) // 2) for t in range(TB)]
    turns = [P * (n * TB - n * (n - 1) // 2) for n in range(TB)]
    chunks = [[(0, t) for t in range(0, 4)], [(1, t) for t in range(1, 4)], [(2, 2), (2, 3), (3, 3)]]
    assert TB == 4
    with ExitStack() as ctx:
        s = Stage(nc, ctx, name)
        qe, ke = (s.sb(n, [P, TB * GH, 4, HD0], F32R) for n in ("qe", "ke"))
        ake = s.sb("ake", [GH * AK, GH, 4, HD0], F32R)
        qt, kt = (s.sb(n, [P, PAIRS, T], F32R) for n in ("qt", "kt"))
        akt = s.sb("akt", [P, PAIRS, 2 * AK], F32R)
        vzh, vzl = (s.sb(n, [P, (TB - 1) * GH * P + GH * SLOT], F32R) for n in ("vzh", "vzl"))
        avh, avl = s.sb("avh", [GH * AK, P], F32R), s.sb("avl", [GH * AK, P], F32R)
        prob = [s.sb(f"prob{n}", [P, TRI * P]) for n in range(2)]
        pth = [s.sb(f"pth{n}", [P, TRI * P], F32R) for n in range(2)]
        ptl = [s.sb(f"ptl{n}", [P, TRI * P], F32R) for n in range(2)]
        nmax, rsum, rinv = (s.sb(n, [P, 2 * TB]) for n in ("nmax", "rsum", "rinv"))
        NAG = TB * GH
        amax, asum, ainv, ginv = (s.sb(n, [P, NAG]) for n in ("amax", "asum", "ainv", "ginv"))
        asub, aprob = (s.sb(n, [P, NAG, AK]) for n in ("asub", "aprob"))
        aexp = asub
        avb = asub[0:GH * AK, :, :].rearrange("p n k -> p (n k)")[:, 0:P]
        aph, apl = ake[:, :, :, :].rearrange("p h s d -> p (h s d)"), s.sb("apl", [GH * AK, T], F32R)
        identb, causal = s.sb("identb", [P, P], BF16), s.sb("causal", [P, P], BF16)
        pairmask, headmask, gating = s.sb("pairmask", [P, 2 * AK]), s.sb("headmask", [GH * AK, P]), s.sb("gating", [P, 1])
        maskf = prob[0][:, 0:P]
        score = [s.ps(f"score{n}", [P, 512]) for n in range(TB)]
        turned = [s.ps(f"turned{n}", [P, 512]) for n in range(2)]
        small, outp = s.ps("small", [P, 512]), s.ps("outp", [P, 512])
        c_loaded, c_ready, zeroed = s.sem("c_loaded"), s.sem("c_ready"), s.sem("zeroed")
        qe_hi, qe_lo, ke_hi, ke_lo, ake_hi, ake_lo = (s.sem(n) for n in ("qe_hi", "qe_lo", "ke_hi", "ke_lo", "ake_hi", "ake_lo"))
        vz_hi, vz_lo, av_step = s.sem("vz_hi"), s.sem("vz_lo"), s.sem("av_step")
        turned_ready = s.sem("turned_ready")
        pair_copied = [s.sem("q_copied"), s.sem("k_copied")]
        small_ready, akt_ready = s.sem("small_ready"), s.sem("akt_ready")
        score_ready, nmax_ready, exp_ready, rinv_ready, norm_ready = (s.sem(n) for n in ("score_ready", "nmax_ready", "exp_ready", "rinv_ready", "norm_ready"))
        pth_ready, ptl_ready, pv_done = s.sem("pth_ready"), s.sem("ptl_ready"), s.sem("pv_done")
        astep, asub_ready, aexp_ready, aprob_ready, aph_ready, apl_ready = (s.sem(n) for n in ("astep", "asub_ready", "aexp_ready", "aprob_ready", "aph_ready", "apl_ready"))
        out_ready, ohi_ready, olo_ready = s.sem("out_ready"), s.sem("ohi_ready"), s.sem("olo_ready")
        NCONST = 5
        QK = 2 * PAIRS
        TURNS = QK + 3 * GH
        ADAPTER_AT, ADAPTER_TURN_AT = 1, 4
        flat = lambda a: a[:, :, :, :].rearrange("p n s d -> p (n s d)")
        slots = lambda a, n: a[:, :, n, :]
        xh, xl = (a[:, :, :].rearrange("p k n -> p (k n)") for a in (xhi, xlo))

        def group(a, bg):
            return a[:, bass.ds(bg, 1), :, :].rearrange("p a t (h d) -> p (a t h) d", d=HD0)

        def diagonal(a, t):
            return a[:, t * GH * P:t * GH * P + GH * SLOT].rearrange("p (h w) -> p h w", w=SLOT)[:, :, 0:HD0]

        with nc.Block() as block:

            @block.sync
            def _(sp):
                for tile, src in ((maskf, "causal"), (pairmask[:, :], "pairmask"), (headmask[:, :], "headmask"), (gating[:, :], "gating")):
                    sp.dma_start(tile, dram[src]).then_inc(c_loaded, 16)

            @block.tensor
            def _(pe):
                def body(bg):
                    def turn_pair(n):
                        p, which = divmod(n, 2)
                        src = flat((qe, ke)[which])
                        if n >= 2:
                            wait(pe, pair_copied[which], PAIRS * bg + p)
                        else:
                            wait(pe, ptl_ready, 3 * GH * bg)
                        for t in range(TB):
                            at = (t * GH + 2 * p) * 4 * HD0
                            last = pe.transpose(turned[n % 2][:, t * P:(t + 1) * P], src[:, at:at + P].bitcast(F32), ident[:, :])
                        last.then_inc(turned_ready, 1)

                    def scores(j, t):
                        rows = slice((j % 2) * 64, (j % 2) * 64 + 64)
                        n = 4 * j + t
                        if t == 0 and j % 2 == 0:
                            for c in pair_copied:
                                wait(pe, c, PAIRS * bg + j // 2 + 1)
                        wait(pe, exp_ready, 4 * GH * bg + max(n - 3, 0))
                        pe.matmul(score[t][:, 0:(t + 1) * P], qt[rows, j // 2, t * P:(t + 1) * P], kt[rows, j // 2, 0:(t + 1) * P],
                                  start=True, stop=False)
                        pe.matmul(score[t][:, t * P:(t + 1) * P], identb[:, :], causal[:, :], start=False, stop=True).then_inc(score_ready, 1)

                    def turn(j, c):
                        m = 3 * j + c
                        wait(pe, norm_ready, 4 * GH * bg + 4 * j + 4)
                        if m < 2:
                            wait(pe, pair_copied[m], PAIRS * (bg + 1))
                        else:
                            wait(pe, ptl_ready, 3 * GH * bg + m - 1)
                        for n, (kn, t) in enumerate(chunks[c]):
                            at = starts[t] + kn * P
                            last = pe.transpose(turned[m % 2][:, n * P:(n + 1) * P], prob[j % 2][:, at:at + P], ident[:, :])
                        last.then_inc(turned_ready, 1)

                    def values(j):
                        wait(pe, pth_ready, 3 * GH * bg + 3 * j + 3)
                        wait(pe, ptl_ready, 3 * GH * bg + 3 * j + 3)
                        for n in range(TB):
                            cols, vals = slice(turns[n], turns[n] + (TB - n) * P), slice((n * GH + j) * P, (n * GH + j + 1) * P)
                            last = three_passes(pe, outp[:, n * P:T], vzh[:, vals], vzl[:, vals], pth[j % 2][:, cols], ptl[j % 2][:, cols],
                                                j == 0 and n == 0, False)
                        last.then_inc(pv_done, 1)

                    wait(pe, qe_lo, 2 * (bg + 1))
                    wait(pe, ke_lo, 2 * (bg + 1))
                    for n in range(QK):
                        turn_pair(n)
                    wait(pe, ake_lo, 2 * (bg + 1))
                    wait(pe, apl_ready, bg)
                    asrc = flat(ake)
                    for p in range(PAIRS):
                        last = pe.transpose(small[:, p * GH * AK:(p + 1) * GH * AK], asrc[:, p * P:(p + 1) * P].bitcast(F32), ident[0:GH * AK, 0:GH * AK])
                    last.then_inc(small_ready, 1)
                    for j in range(GH):
                        for t in range(TB):
                            scores(j, t)
                        if j == ADAPTER_AT:
                            wait(pe, akt_ready, bg + 1)
                            for t in range(TB):
                                for p in range(PAIRS):
                                    at = t * GH * AK + p * 2 * AK
                                    last = pe.matmul(small[:, at:at + 2 * AK], qt[:, p, t * P:(t + 1) * P], akt[:, p, :], start=True, stop=True)
                            last.then_inc(small_ready, 1)
                        if j == ADAPTER_TURN_AT:
                            wait(pe, aprob_ready, bg + 1)
                            for t in range(TB):
                                last = pe.transpose(small[0:GH * AK, t * P:(t + 1) * P],
                                                    aprob[:, t * GH:(t + 1) * GH, :].rearrange("p h k -> p (h k)"), ident[:, :])
                            last.then_inc(small_ready, 1)
                        if j == 2:
                            wait(pe, vz_lo, TB * (bg + 1))
                            wait(pe, olo_ready, bg)
                        if j >= 2:
                            values(j - 2)
                        if j >= 1:
                            for c in range(3):
                                turn(j - 1, c)
                    values(GH - 2)
                    for c in range(3):
                        turn(GH - 1, c)
                    values(GH - 1)
                    wait(pe, apl_ready, bg + 1)
                    wait(pe, av_step, 3 * (bg + 1))
                    three_passes(pe, outp[:, :], avh[:, :], avl[:, :], aph, apl[:, :], False, True).then_inc(out_ready, 1)

                wait(pe, c_ready, 2)
                peeled(pe, NG0 * B, body)

            @block.scalar
            def _(act):
                def body(bg):
                    def turned_split(j, c):
                        m, w = 3 * j + c, P * len(chunks[c])
                        at = turns[min(c, 2)]
                        wait(act, turned_ready, TURNS * bg + QK + m + 1)
                        if j >= 2 and c == 0:
                            wait(act, pv_done, GH * bg + j - 1)
                        act.activation(pth[j % 2][:, at:at + w], turned[m % 2][:, 0:w], ACT.Copy).then_inc(pth_ready, 1)

                    wait(act, turned_ready, TURNS * bg)
                    wait(act, small_ready, 3 * bg)
                    for n, (dst, src, sem, at) in enumerate(((qe, q, qe_hi, (0, 2)), (ke, k, ke_hi, (0, 1)))):
                        for slot in at:
                            act.activation(slots(dst, slot), group(src, bg), ACT.Copy).then_inc(sem, 1)
                    for slot in (0, 1):
                        act.activation(slots(ake, slot), ak[:, bass.ds(bg // B, 1), :].rearrange("p a (h d) -> p (a h) d", d=HD0), ACT.Copy).then_inc(ake_hi, 1)
                    wait(act, out_ready, bg)
                    for t in range(TB):
                        act.activation(diagonal(vzh, t), v[:, bass.ds(bg, 1), t, :].rearrange("p a (h d) -> p (a h) d", d=HD0), ACT.Copy).then_inc(vz_hi, 1)
                    for p in range(PAIRS):
                        wait(act, turned_ready, TURNS * bg + 2 * p + 1)
                        act.activation(qt[:, p, :], turned[0][:, :], ACT.Copy).then_inc(pair_copied[0], 1)
                    for j in range(GH):
                        for t in range(TB):
                            slot, n = j % 2 * TB + t, 4 * j + t
                            w = (t + 1) * P
                            wait(act, nmax_ready, 4 * GH * bg + n + 1)
                            act.activation(prob[j % 2][:, starts[t]:starts[t] + w], score[t][:, 0:w], ACT.Exp, bias=nmax[:, slot:slot + 1],
                                           accum_out=rsum[:, slot:slot + 1]).then_inc(exp_ready, 1)
                        if j == ADAPTER_AT + 1:
                            wait(act, asub_ready, bg + 1)
                            act.activation(aexp[:, :, :], asub[:, :, :], ACT.Exp, scale=float(HD0 ** 0.5 / C ** 0.5)).then_inc(aexp_ready, 1)
                        if j == ADAPTER_TURN_AT + 1:
                            wait(act, small_ready, 3 * bg + 3)
                            act.activation(aph, small[0:GH * AK, :], ACT.Copy).then_inc(aph_ready, 1)
                        if j >= 1:
                            for c in range(3):
                                turned_split(j - 1, c)
                    for c in range(3):
                        turned_split(GH - 1, c)
                    wait(act, out_ready, bg + 1)
                    act.activation(xh[:, bass.ds(bg * T, T)], outp[:, :], ACT.Copy).then_inc(ohi_ready, 1)

                wait(act, zeroed, 2)
                peeled(act, NG0 * B, body)

            @block.gpsimd
            def _(pool):
                wait(pool, c_loaded, 16 * 4)
                pool.tensor_copy(causal[:, :], maskf).then_inc(c_ready, 1)
                pool.tensor_copy(identb[:, :], ident[:, :]).then_inc(c_ready, 1)
                with pool.Fori(0, NG0 * B) as bg:
                    for j in range(GH):
                        wait(pool, rinv_ready, GH * bg + j + 1)
                        for t in range(TB):
                            slot, w = j % 2 * TB + t, (t + 1) * P
                            part = prob[j % 2][:, starts[t]:starts[t] + w]
                            pool.tensor_tensor(part, part, rinv[:, slot:slot + 1].broadcast_to([P, w]), ALU.mult).then_inc(norm_ready, 1)

            @block.vector
            def _(dve):
                def body(bg):
                    def turned_split(j, c):
                        m, w = 3 * j + c, P * len(chunks[c])
                        at = turns[min(c, 2)]
                        wait(dve, pth_ready, 3 * GH * bg + m + 1)
                        dve.tensor_tensor(ptl[j % 2][:, at:at + w], turned[m % 2][:, 0:w], pth[j % 2][:, at:at + w], ALU.subtract).then_inc(ptl_ready, 1)

                    def adapter_softmax():
                        grp = small[:, 0:NAG * AK].rearrange("p (n k) -> p n k", k=AK)
                        wait(dve, small_ready, 3 * bg + 2)
                        dve.tensor_reduce(amax[:, :], grp, AX, ALU.max).then_inc(astep, 1)
                        wait(dve, astep, 4 * bg + 1)
                        dve.tensor_tensor(asub[:, :, :], grp, spread(amax[:, :], [P, NAG, AK]), ALU.subtract).then_inc(asub_ready, 1)

                    def adapter_norm():
                        wait(dve, aexp_ready, bg + 1)
                        dve.tensor_reduce(asum[:, :], aexp[:, :, :], AX, ALU.add).then_inc(astep, 1)
                        wait(dve, astep, 4 * bg + 2)
                        dve.reciprocal(ainv[:, :], asum[:, :]).then_inc(astep, 1)
                        wait(dve, astep, 4 * bg + 3)
                        dve.tensor_scalar(ginv[:, :], ainv[:, :], gating[:, 0:1], None, ALU.mult).then_inc(astep, 1)
                        wait(dve, astep, 4 * bg + 4)
                        dve.tensor_tensor(aprob[:, :, :], aexp[:, :, :], spread(ginv[:, :], [P, NAG, AK]), ALU.mult).then_inc(aprob_ready, 1)

                    for dst, src, hi, lo, at in ((qe, q, qe_hi, qe_lo, (1, 3)), (ke, k, ke_hi, ke_lo, (2, 3))):
                        wait(dve, hi, 2 * bg + 2)
                        for slot in at:
                            dve.tensor_tensor(slots(dst, slot), group(src, bg), slots(dst, 0), ALU.subtract).then_inc(lo, 1)
                    wait(dve, ake_hi, 2 * bg + 2)
                    for slot in (2, 3):
                        dve.tensor_tensor(slots(ake, slot), ak[:, bass.ds(bg // B, 1), :].rearrange("p a (h d) -> p (a h) d", d=HD0),
                                          slots(ake, 0), ALU.subtract).then_inc(ake_lo, 1)
                    for p in range(PAIRS):
                        wait(dve, turned_ready, TURNS * bg + 2 * p + 2)
                        dve.tensor_copy(kt[:, p, :], turned[1][:, :]).then_inc(pair_copied[1], 1)
                    wait(dve, small_ready, 3 * bg + 1)
                    dve.tensor_tensor(akt[:, :, :], small[:, 0:PAIRS * GH * AK].rearrange("p (a n) -> p a n", a=PAIRS)[:, :, 0:2 * AK],
                                      pairmask[:, :].unsqueeze(1).broadcast_to([P, PAIRS, 2 * AK]), ALU.mult).then_inc(akt_ready, 1)
                    for t in range(TB):
                        wait(dve, vz_hi, TB * bg + t + 1)
                        dve.tensor_tensor(diagonal(vzl, t), v[:, bass.ds(bg, 1), t, :].rearrange("p a (h d) -> p (a h) d", d=HD0),
                                          diagonal(vzh, t), ALU.subtract).then_inc(vz_lo, 1)
                    wait(dve, out_ready, bg)
                    dve.tensor_tensor(avb, av[:, bass.ds(bg // B, 1), :].rearrange("p a f -> p (a f)"), headmask[:, :], ALU.mult).then_inc(av_step, 1)
                    wait(dve, av_step, 3 * bg + 1)
                    dve.tensor_copy(avh[:, :], avb).then_inc(av_step, 1)
                    wait(dve, av_step, 3 * bg + 2)
                    dve.tensor_tensor(avl[:, :], avb, avh[:, :], ALU.subtract).then_inc(av_step, 1)
                    for j in range(GH):
                        for t in range(TB):
                            slot, n = j % 2 * TB + t, 4 * j + t
                            wait(dve, score_ready, 4 * GH * bg + n + 1)
                            dve.tensor_reduce(nmax[:, slot:slot + 1], score[t][:, 0:(t + 1) * P], AX, ALU.max, negate=True).then_inc(nmax_ready, 1)
                        slot = j % 2 * TB
                        wait(dve, exp_ready, 4 * GH * bg + 4 * j + 4)
                        dve.reciprocal(rinv[:, slot:slot + TB], rsum[:, slot:slot + TB]).then_inc(rinv_ready, 1)
                        if j == ADAPTER_AT + 1:
                            adapter_softmax()
                        if j == ADAPTER_AT + 2:
                            adapter_norm()
                        if j == ADAPTER_TURN_AT + 1:
                            wait(dve, aph_ready, bg + 1)
                            dve.tensor_tensor(apl[:, :], small[0:GH * AK, :], aph, ALU.subtract).then_inc(apl_ready, 1)
                        if j >= 1:
                            for c in range(3):
                                turned_split(j - 1, c)
                    for c in range(3):
                        turned_split(GH - 1, c)
                    wait(dve, ohi_ready, bg + 1)
                    dve.tensor_tensor(xl[:, bass.ds(bg * T, T)], outp[:, :], xh[:, bass.ds(bg * T, T)], ALU.subtract).then_inc(olo_ready, 1)

                for a in (vzh, vzl):
                    dve.memset(a[:, :].bitcast(F32), 0.0).then_inc(zeroed, 1)
                wait(dve, zeroed, 2)
                wait(dve, c_loaded, 16 * 4)
                peeled(dve, NG0 * B, body)


def projection_block(nc, env, dram, name):
    x, xhi, xlo = env["x"], env["xhi"], env["xlo"]
    with ExitStack() as ctx:
        s = Stage(nc, ctx, name)
        raw, whi, wlo = s.sb("raw", [P, KC, C]), s.sb("whi", [P, KC, C], F32R), s.sb("wlo", [P, KC, C], F32R)
        bank = [s.ps(f"bank{n}", [P, C]) for n in range(4)]
        loaded, whi_ready, wlo_ready, out_ready, added = (s.sem(n) for n in ("loaded", "whi_ready", "wlo_ready", "out_ready", "added"))
        with nc.Block() as block:

            @block.sync
            def _(sp):
                sp.dma_start(raw[:, :, :], dram["w_proj"]).then_inc(loaded, 16)

            @block.scalar
            def _(act):
                act.wait_ge(loaded, 16)
                act.activation(whi[:, :, :], raw[:, :, :], ACT.Copy).then_inc(whi_ready, 1)

            @block.tensor
            def _(pe):
                pe.wait_ge(wlo_ready, 1)
                for t in range(NT):
                    if t >= 4:
                        pe.wait_ge(added, t - 3)
                    tok = slice(t * P, (t + 1) * P)
                    for k in range(KC):
                        last = three_passes(pe, bank[t % 4][:, :], xhi[:, k, tok], xlo[:, k, tok], whi[:, k, :], wlo[:, k, :],
                                            k == 0, k == KC - 1)
                    last.then_inc(out_ready, 1)

            @block.vector
            def _(dve):
                dve.wait_ge(whi_ready, 1)
                dve.tensor_tensor(wlo[:, :, :], raw[:, :, :], whi[:, :, :], ALU.subtract).then_inc(wlo_ready, 1)
                for t in range(NT):
                    dve.wait_ge(out_ready, t + 1)
                    dve.tensor_tensor(x[:, t, :], bank[t % 4][:, :], x[:, t, :], ALU.add).then_inc(added, 1)


def store_stage(nc, env, out):
    with ExitStack() as ctx:
        s = Stage(nc, ctx, "store")
        stored = s.sem("stored")
        with nc.Block() as block:

            @block.sync
            def _(sp):
                sp.dma_start(out.rearrange("(t p) c -> p t c", p=P), env["x"][:, :, :]).then_inc(stored, 16)
                sp.wait_ge(stored, 16)


def macaron_kernel(nc, dram, out, stages=None):
    with ExitStack() as ctx:
        s = Stage(nc, ctx, "all")
        env = {"x": s.sb("x", [P, NT, C]), "ident": s.sb("ident", [P, P]),
               "xhi": s.sb("xhi", [P, KC, NT * P], F32R), "xlo": s.sb("xlo", [P, KC, NT * P], F32R)}
        Stage.used = []
        load_stage(nc, env, dram)
        for n, stage in enumerate((lime_ffn_stage, adapter_attention_stage, lime_ffn_stage, moe_stage, gqa_stage, moe_stage)):
            if stages is None or n in stages:
                layernorm_stage(nc, env, f"ln{n}")
                stage(nc, env, dram, f"st{n}")
            if n == 2:
                Stage.recycle(nc)
        store_stage(nc, env, out)


def constants():
    f = np.float32
    causal = np.where(np.arange(P)[None, :] <= np.arange(P)[:, None], f(0), f(-3e38)).astype(f)
    theta = (f(1) / f(10000.0) ** (np.arange(0, HD0, 2, dtype=f) / f(HD0))).astype(f)
    angle = np.outer(np.arange(T, dtype=f), theta).astype(f)
    angle = np.concatenate([angle, angle], 1).astype(np.float64)
    sign = np.where(np.arange(HD0) < HD0 // 2, -1.0, 1.0)
    cos, sin = np.cos(angle), np.sin(angle) * sign
    rope = np.stack([cos * 0.25, sin * 0.25, cos, sin]).astype(f).reshape(4, TB, P, HD0).transpose(2, 0, 1, 3)
    rows = np.arange(P)[:, None]
    return {
        "ident": np.eye(P, dtype=f),
        "pair": (rows == (np.arange(P)[None, :] | 1)).astype(f),
        "odd": np.stack([np.arange(P) % 2, -(np.arange(P) % 2)], 1).astype(f),
        "expert": np.broadcast_to(np.arange(E1, dtype=f), (P, E1)),
        "causal": causal,
        "rope": rope,
        "pairmask": (rows // 64 == np.arange(2 * AK)[None, :] // AK).astype(f),
        "headmask": (np.arange(GH * AK)[:, None] // AK == np.arange(P)[None, :] // HD0).astype(f),
    }


def layout(a):
    def chunked(w):
        return w.T.reshape(-1, P, w.shape[0]).transpose(1, 0, 2)

    gate_up, down = a["L1_ffn_w_gate_up"], a["L1_ffn_w_down"]
    sgu, sdn = a["L1_ffn_shared_w_gate_up"], a["L1_ffn_shared_w_down"]
    units = [np.concatenate([chunked(gate_up[e]).reshape(P, -1), down[e].T], 1) for e in range(E1)]
    for n in range(SI // MI):
        gu = np.concatenate([sgu[n * MI:(n + 1) * MI], sgu[SI + n * MI:SI + (n + 1) * MI]], 0)
        units.append(np.concatenate([chunked(gu).reshape(P, -1), sdn[:, n * MI:(n + 1) * MI].T], 1))
    wq, wk, wv, wo = (a["L1_attn_" + n] for n in ("wq", "wk", "wv", "wo"))
    kv = [chunked(np.concatenate([wk[g * D1:(g + 1) * D1], wv[g * D1:(g + 1) * D1]], 0)).reshape(P, -1) for g in range(KV1)]
    qs = [np.concatenate([chunked(wq[h * D1:(h + 1) * D1]).reshape(P, -1) for h in range(g * G1, (g + 1) * G1)], 1) for g in range(KV1)]
    os = [np.concatenate([wo[:, h * D1:(h + 1) * D1].T for h in range(g * G1, (g + 1) * G1)], 1) for g in range(KV1)]
    prefix = np.concatenate([a["L0_attn_adapter_wte"]] * GH, 0)
    return {
        "x": a["L0_attn_x"].reshape(B * T, C),
        "w0": chunked(np.concatenate([a["L0_ffn_W"], a["L0_ffn_A"].T], 0)),
        "a_t": a["L0_ffn_A"].T, "l_t": a["L0_ffn_LiMEs"].T, "lime": a["L0_ffn_LiMEs"], "bmat": a["L0_ffn_Bmat"],
        "bias": np.broadcast_to(a["L0_ffn_b"], (P, C)),
        "w_attn": chunked(a["L0_attn_w_attn"]), "w_proj": chunked(a["L0_attn_w_proj"]),
        "prefix": chunked(prefix), "gating": np.broadcast_to(a["L0_attn_gating"], (P, 1)),
        "gate_w": chunked(a["L1_ffn_gate_w"]), "moe_w": np.stack(units),
        "gqa_kv": np.stack(kv), "gqa_q": np.stack(qs), "gqa_o": np.stack(os),
        **constants(),
    }


def kernel(**inputs):
    import concourse.bacc as bacc
    from concourse.bass_utils import run_bass_kernel_spmd

    nc = bacc.Bacc("TRN2", target_bir_lowering=False, num_devices=1)
    arrays = {f"in_{n}": np.ascontiguousarray(v) for n, v in layout({k: np.asarray(v) for k, v in inputs.items()}).items()}
    dram = {n[3:]: nc.dram_tensor(n, v.shape, mybir.dt.from_np(v.dtype), kind="ExternalInput").ap() for n, v in arrays.items()}
    out = nc.dram_tensor("out", (B * T, C), F32, kind="ExternalOutput").ap()
    macaron_kernel(nc, dram, out)
    r = run_bass_kernel_spmd(nc, [arrays], core_ids=[0])
    return r.results[0]["out"].reshape(B, T, C)
```
